# Optimizing a Trainium2 kernel written in Bass

```python
import numpy as np
import jax
import jax.numpy as jnp

def _softmax(x, axis=-1):
    return jax.nn.softmax(x, axis=axis)

def _gelu(x):
    return jax.nn.gelu(x, approximate=True)

def _silu(x):
    return jax.nn.silu(x)

def _sigmoid(x):
    return jax.nn.sigmoid(x)

def _layernorm(x, axis=-1, eps=1e-05):
    m = jnp.mean(x, axis=axis, keepdims=True)
    v = jnp.var(x, axis=axis, keepdims=True)
    return (x - m) / jnp.sqrt(v + eps)

def _scatter_add(tgt, idx, src, axis=0):
    return tgt.at[idx].add(src)

def _segment_sum(src, seg, n):
    return jax.ops.segment_sum(src, seg, n)
kernel_name = 'mk_adj_resnorm_d2_adj_r2_de5e19'

def setup_inputs(seed: int=0):
    np.random.seed(seed)
    _w = jnp.asarray

    def _rec_inputs():
        import jax
        import jax.numpy as jnp
        _gk = jax.random.key(seed)
        x = -9.806e-05 + 1 * jax.random.normal(jax.random.fold_in(_gk, 1), (2048, 64), jnp.float32)
        _a = jax.random.bernoulli(jax.random.fold_in(_gk, 2), 0.000976562, (2048, 2048))
        _af = _a.astype(jnp.float32)
        adj = _af
        return (x, adj)
    x, adj = _rec_inputs()

    def _L0_gnn_setup():
        import jax, jax.numpy as jnp
        import numpy as np
        N, D_IN, D_OUT = (4096, 64, 64)
        MAX_NEIGH = 100
        DECAY = 0.5
        key = jax.random.key(seed)
        k1, k2, k3, k4 = jax.random.split(key, 4)
        stdv = 1.0 / np.sqrt(D_OUT)
        inputs = {'input': jax.random.normal(k1, (N, D_IN), dtype=jnp.float32), 'adj': jax.random.randint(k2, (N, N), 0, 2).astype(jnp.float32), 'weight': jax.random.uniform(k3, (D_IN, D_OUT), minval=-stdv, maxval=stdv, dtype=jnp.float32), 'bias': jax.random.uniform(k4, (D_OUT,), minval=-stdv, maxval=stdv, dtype=jnp.float32)}
        return inputs
    _L0_gnn_all = _L0_gnn_setup()
    _L0_gnn_in = {k: v for k, v in _L0_gnn_all.items() if k in ('weight', 'bias')}
    del _L0_gnn_all

    def _L1_gnn_setup():
        import jax, jax.numpy as jnp
        import numpy as np
        N, D_IN, D_OUT = (8192, 64, 64)
        AVG_DEG = 32.0
        L2_EPS = 1e-12
        key = jax.random.key(seed)
        kx, ka, kw, kb = jax.random.split(key, 4)
        X = jax.random.normal(kx, (N, D_IN), dtype=jnp.float32)
        adj = (jax.random.uniform(ka, (N, N)) < AVG_DEG / N).astype(jnp.float32)
        bound = 1.0 / np.sqrt(2 * D_IN)
        W = jax.random.uniform(kw, (2 * D_IN, D_OUT), dtype=jnp.float32, minval=-bound, maxval=bound)
        b = jax.random.uniform(kb, (D_OUT,), dtype=jnp.float32, minval=-bound, maxval=bound)
        return {'X': X, 'adj': adj, 'W': W, 'b': b}
    _L1_gnn_all = _L1_gnn_setup()
    _L1_gnn_in = {k: v for k, v in _L1_gnn_all.items() if k in ('W', 'b')}
    del _L1_gnn_all
    return {'x': x, 'adj': adj, 'L0_gnn_weight': _L0_gnn_in['weight'], 'L0_gnn_bias': _L0_gnn_in['bias'], 'L1_gnn_W': _L1_gnn_in['W'], 'L1_gnn_b': _L1_gnn_in['b']}

def reference(x, adj, L0_gnn_weight, L0_gnn_bias, L1_gnn_W, L1_gnn_b):
    import jax
    import jax.numpy as jnp

    def _L0_gnn_ref(input, adj, weight, bias):
        import jax, jax.numpy as jnp
        import numpy as np
        N, D_IN, D_OUT = (4096, 64, 64)
        MAX_NEIGH = 100
        DECAY = 0.5
        support = input @ weight
        mask = (adj != 0).astype(support.dtype)
        rank = jnp.cumsum(mask, axis=1)
        deg = rank[:, -1:]
        k = jnp.minimum(deg, float(MAX_NEIGH))
        pos = rank - (deg - k)
        w = mask * jnp.where(pos > 0, DECAY ** (k - pos), 0.0)
        out = w @ support + bias
        return out

    def _L1_gnn_ref(X, adj, W, b):
        import jax, jax.numpy as jnp
        import numpy as np
        N, D_IN, D_OUT = (8192, 64, 64)
        AVG_DEG = 32.0
        L2_EPS = 1e-12
        deg = jnp.clip(jnp.sum(adj, axis=1, keepdims=True) + 1.0, 1.0, None)
        h_neigh = (adj @ X + X) / deg
        concat = jnp.concatenate([X, h_neigh], axis=1)
        z = concat @ W + b
        out = jax.nn.relu(z)
        norm = jnp.linalg.norm(out, axis=1, keepdims=True)
        return out / jnp.maximum(norm, L2_EPS)
    x = _layernorm(x + _L0_gnn_ref(x, adj, L0_gnn_weight, L0_gnn_bias), axis=-1)
    x = _layernorm(x + _L1_gnn_ref(x, adj, L1_gnn_W, L1_gnn_b), axis=-1)
    return x

_drawn_inputs = setup_inputs


def setup_inputs(seed=0):
    import zlib

    import numpy as np

    out = dict(_drawn_inputs(seed))
    spreads = {}
    factors = {'L1_gnn_b': 3.942}
    for name, (base, spread) in spreads.items():
        noise = np.random.default_rng([zlib.crc32(name.encode()), seed]).standard_normal(out[name].shape)
        drawn = base * np.exp(spread * noise) if base else spread * noise
        out[name] = jnp.asarray(drawn.astype(out[name].dtype))
    for name, factor in factors.items():
        out[name] = (out[name] * factor).astype(out[name].dtype)
    return out
```

```python
from contextlib import ExitStack

import concourse.bass as bass
from concourse import mybir

P = 128
N, D = 2048, 64
NB = N // P
PARTS = 3
PD = PARTS * D
CH = 512
RT = CH // P
PAIRS = N // (2 * CH)
QB = 4
UNITS = 2 * NB // QB
RING = 8
TS = 256
NEIGH = 100
EXP1 = 128
LN_EPS = 1e-5
SS_MIN = 1e-24
SUP_SCALE = 2.0 ** (127 - NEIGH)

ALU = mybir.AluOpType
ACT = mybir.ActivationFunctionType
AX_X = mybir.AxisListType.X
F32 = mybir.dt.float32
BF16 = mybir.dt.bfloat16
I16 = mybir.dt.int16


def build(nc, x, adj, w0, b0, w1, b1, out):
    with ExitStack() as ctx:
        def sb(name, shape, dt):
            return ctx.enter_context(nc.sbuf_tensor(name, shape, dt))

        def psum(name, shape, dt):
            return ctx.enter_context(nc.psum_tensor(name, shape, dt))

        def sem(name):
            return ctx.enter_context(nc.semaphore(name))

        stage = sb("stage", [P, RING, RT, QB * P], F32)
        adjT = sb("adjT", [P, NB, N], BF16)
        wts = sb("wts", [P, 2, 2, CH], BF16)
        xs = sb("xs", [P, NB, D], F32)
        xb = sb("xb", [P, NB, D], F32)
        xT = sb("xT", [P, NB // 2, P], F32)
        sup32 = sb("sup32", [P, NB, D], F32)
        sup = sb("sup", [P, NB, PD], BF16)
        x1 = sb("x1", [P, NB, D], F32)
        x1T = sb("x1T", [P, NB // 2, P], F32)
        yu = sb("yu", [P, NB, 2, D], F32)
        ysp = sb("ysp", [P, NB, PD + 2], BF16)
        suffix = sb("suffix", [P, P], BF16)
        rest = sb("rest", [P, P], BF16)
        ident16 = sb("ident16", [P, P], BF16)
        ident32 = sb("ident32", [P, P], F32)
        wd0 = sb("wd0", [P, 2, D], F32)
        wd1 = sb("wd1", [P, 2, 2, D], F32)
        b0row = sb("b0row", [P, D], F32)
        b1row = sb("b1row", [P, D], F32)
        t0 = sb("t0", [P, RT, D], F32)
        t1 = sb("t1", [P, RT, D], F32)
        t2 = sb("t2", [P, RT, D], F32)
        col = sb("col", [P, 8, RT], F32)
        outs = sb("outs", [P, NB, D], F32)

        acc = psum("acc", [P, 2 * RT, TS], F32)
        tmp = psum("tmp", [P, 2, CH], F32)
        cnt = psum("cnt", [P, 2, CH], F32)

        x_loaded = sem("x_loaded")
        par_loaded = sem("par_loaded")
        adj_loaded = [sem(f"adj_loaded{i}") for i in range(RING)]
        zeroed = sem("zeroed")
        consts = sem("consts")
        tmp_full = sem("tmp_full")
        tmp_read = sem("tmp_read")
        cnt_done = [sem(f"cnt_done{i}") for i in range(2)]
        w_ready = [sem(f"w_ready{i}") for i in range(2)]
        w_used = [sem(f"w_used{i}") for i in range(2)]
        sup_ready = sem("sup_ready")
        acc_read = sem("acc_read")
        x1_ready = sem("x1_ready")
        y_ready = sem("y_ready")
        agg_done = sem("agg_done")
        agg_read = sem("agg_read")
        chain = sem("chain")
        to_act = sem("to_act")
        from_act = sem("from_act")
        out_ready = sem("out_ready")
        stored = sem("stored")

        X_FILLS = 4
        groups = [(p, 7 - k, c) for p in range(PAIRS) for k in range(NB // 2) for c in range(2)]
        fills = [("x", h) for h in range(2)] + [("sup", h) for h in range(2)]
        Y0_AT = 6
        for i, g in enumerate(groups):
            if i == 2 * (NB // 2) + Y0_AT:
                fills += [("x1T", 0), ("x1T", 1), ("yu", 0), ("yu", 1)]
            fills.append(("adj", g))
        fills += [("x1T", 2), ("x1T", 3), ("yu", 2), ("yu", 3)]
        number = {f: i for i, f in enumerate(fills)}

        def unit(p, bp, c):
            return p * UNITS + (NB // QB - 1 - bp // 2) * 2 + c

        def nth(p, b):
            return p * NB + NB - 1 - b

        x_v = x.rearrange("(t p) d -> p t d", p=P)
        out_v = out.rearrange("(t p) d -> p t d", p=P)
        adj_v = adj.rearrange("(c r p) (q n) -> c q p r n", r=RT, p=P, n=QB * P)

        block = ctx.enter_context(nc.Block())

        @block.sync
        def _(sp):
            sp.dma_start(xs[:, :, :], x_v).then_inc(x_loaded, 16)
            for p in range(PAIRS):
                for q in range(NB // QB):
                    for c in range(2):
                        u = p * UNITS + 2 * q + c
                        if u >= RING:
                            v = u - RING
                            old = (v // UNITS, 2 * (NB // QB - 1 - v % UNITS // 2), v % 2)
                            sp.wait_ge(tmp_full, number[("adj", old)] + 1)
                        sp.dma_start(stage[:, u % RING, :, :],
                                     adj_v[2 * p + c, NB // QB - 1 - q]).then_inc(adj_loaded[u % RING], 16)
            for g in range(NB // RT):
                sp.wait_ge(out_ready, g + 1)
                sp.dma_start(out_v[:, g * RT:(g + 1) * RT, :],
                             outs[:, g * RT:(g + 1) * RT, :]).then_inc(stored, 16)
            sp.wait_ge(stored, 16 * (NB // RT))

        @block.gpsimd
        def _(pool):
            nc.gpsimd.memset(suffix[:], -float(EXP1)).then_inc(zeroed, 1)
            nc.gpsimd.memset(rest[:], -float(EXP1)).then_inc(zeroed, 1)
            nc.gpsimd.memset(ident16[:], 0.0).then_inc(zeroed, 1)
            nc.gpsimd.memset(ident32[:], 0.0).then_inc(zeroed, 1)
            nc.gpsimd.memset(wd0[:], 0.0).then_inc(zeroed, 1)
            nc.gpsimd.memset(wd1[:], 0.0).then_inc(zeroed, 1)
            nc.gpsimd.memset(ysp[:, :, PD:PD + 2], 1.0).then_inc(zeroed, 1)
            pool.wait_ge(zeroed, 7)

            def select(t, op, fill, s=1):
                return nc.gpsimd.affine_select(out=t[:, :], in_=t[:, :], compare_op=op, fill=fill, base=0,
                                               pattern=[[-s, P]], channel_multiplier=s)
            select(ident32, ALU.not_equal, 1.0).then_inc(consts, 1)
            select(ident16, ALU.not_equal, 1.0).then_inc(consts, 1)
            select(suffix, ALU.is_ge, 0.0).then_inc(consts, 1)
            select(rest, ALU.is_ge, 0.0, -1).then_inc(consts, 1)
            pool.wait_ge(consts, 4)
            select(suffix, ALU.not_equal, float(EXP1 * NEIGH)).then_inc(consts, 1)
            select(rest, ALU.not_equal, -float(EXP1 * (NEIGH + 1))).then_inc(consts, 1)

        @block.scalar
        def _(act):
            act.wait_ge(zeroed, 7)
            for h in range(2):
                act.dma_start(wd0[h * D:(h + 1) * D, h, :], w0).then_inc(par_loaded, 16)
                act.dma_start(wd1[h * D:(h + 1) * D, h, 0, :], w1[D:2 * D, :]).then_inc(par_loaded, 16)
                act.dma_start(wd1[h * D:(h + 1) * D, h, 1, :], w1[0:D, :]).then_inc(par_loaded, 16)
            act.dma_start(b0row[:, :], b0.partition_broadcast(P)).then_inc(par_loaded, 16)
            act.dma_start(b1row[:, :], b1.partition_broadcast(P)).then_inc(par_loaded, 16)

            def root(n):
                act.wait_ge(to_act, n + 1)
                nc.scalar.activation(col[:, 1, :], col[:, 0, :], ACT.Sqrt).then_inc(from_act, 1)

            for p in range(PAIRS):
                for b in reversed(range(NB)):
                    for c in range(2):
                        n = nth(p, b)
                        act.wait_ge(cnt_done[c], n + 1)
                        if n >= 2:
                            act.wait_ge(w_used[c], n - 1)
                        nc.scalar.activation(wts[:, c, b % 2, :].bitcast(I16), cnt[:, c, :],
                                             ACT.Relu).then_inc(w_ready[c], 1)
                    if p == 1 and b in (15, 14):
                        root(15 - b)
            root(2)
            root(3)
            for g in range(NB // RT):
                root(4 + 2 * g)
                root(5 + 2 * g)

        @block.vector
        def _(dve):
            steps = [0]

            def link(ins):
                steps[0] += 1
                ins.then_inc(chain, 1)
                dve.wait_ge(chain, steps[0])

            roots = [0]

            def tmp_bank(f):
                n = number[f]
                dve.wait_ge(tmp_full, n + 1)
                return tmp[:, n % 2, :]

            def split(src, dst, work):
                link(nc.vector.tensor_copy(dst[:, :, 0:D], src))
                link(nc.vector.tensor_tensor(work, src, dst[:, :, 0:D], ALU.subtract))
                link(nc.vector.tensor_copy(dst[:, :, D:2 * D], work))
                return nc.vector.tensor_tensor(dst[:, :, 2 * D:3 * D], work, dst[:, :, D:2 * D], ALU.subtract)

            def spread(v):
                return v.unsqueeze(2).to_broadcast([P, RT, D])

            def newton_root():
                to = roots[0]
                roots[0] += 1
                dve.wait_ge(from_act, to + 1)
                link(nc.vector.reciprocal(col[:, 2, :], col[:, 1, :]))
                link(nc.vector.tensor_tensor(col[:, 2, :], col[:, 2, :], col[:, 0, :], ALU.mult))
                link(nc.vector.tensor_tensor(col[:, 2, :], col[:, 2, :], col[:, 1, :], ALU.add))
                link(nc.vector.tensor_scalar(col[:, 2, :], col[:, 2, :], 0.5, None, ALU.mult))
                link(nc.vector.reciprocal(col[:, 3, :], col[:, 2, :]))

            def layernorm(src, dst):
                link(nc.vector.reduce_sum(col[:, 4, :], src[:, :, :], AX_X))
                link(nc.vector.scalar_tensor_tensor(out=t2[:, :, :], in0=spread(col[:, 4, :]), scalar=-1.0 / D,
                                                    in1=src[:, :, :], op0=ALU.mult, op1=ALU.add))
                link(nc.vector.tensor_tensor(t1[:, :, :], t2[:, :, :], t2[:, :, :], ALU.mult))
                link(nc.vector.reduce_sum(col[:, 5, :], t1[:, :, :], AX_X))
                nc.vector.tensor_scalar(col[:, 0, :], col[:, 5, :], 1.0 / D, LN_EPS,
                                        ALU.mult, ALU.add).then_inc(to_act, 1)
                newton_root()
                return nc.vector.tensor_tensor(dst, t2[:, :, :], spread(col[:, 3, :]), ALU.mult)

            def finish_layer0(ch):
                c, t = ch % 2, ch * RT
                sums = acc[:, c * RT:(c + 1) * RT, 0:PD].rearrange("p t (k d) -> p t d k", k=PARTS)
                dve.wait_ge(w_used[c], (ch // 2 + 1) * NB)
                nc.vector.reduce_sum(t0[:, :, :], sums, AX_X).then_inc(acc_read, 1)
                dve.wait_ge(acc_read, ch + 1)
                link(nc.vector.tensor_tensor(t0[:, :, :], t0[:, :, :], xb[:, t:t + RT, :], ALU.add))
                layernorm(t0, x1[:, t:t + RT, :]).then_inc(x1_ready, 1)

            def x1_transposed(ch):
                bank = tmp_bank(("x1T", ch))
                nc.vector.tensor_copy(x1T[:, 2 * ch:2 * ch + 2, :],
                                      bank[:, 0:2 * P].rearrange("p (k n) -> p k n", k=2)).then_inc(tmp_read, 1)

            def layer1_products(ch):
                bank = tmp_bank(("yu", ch))
                t = ch * RT
                yv = yu[:, t:t + RT, :, :]
                nc.vector.tensor_copy(yv, bank.rearrange("p (t s d) -> p t s d", t=RT, s=2)).then_inc(tmp_read, 1)
                dve.wait_ge(tmp_read, number[("yu", ch)] + 1)
                split(yu[:, t:t + RT, 0, :], ysp[:, t:t + RT, :], t0[:, :, :]).then_inc(y_ready, 1)
                link(nc.vector.tensor_tensor(yu[:, t:t + RT, 1, :], yu[:, t:t + RT, 1, :],
                                             b1row[:, :].unsqueeze(1).to_broadcast([P, RT, D]), ALU.add))

            for h in range(2):
                bank = tmp_bank(("x", h))
                nc.vector.tensor_copy(xT[:, 4 * h:4 * h + 4, :],
                                      bank.rearrange("p (k n) -> p k n", k=4)).then_inc(tmp_read, 1)
            for h in range(2):
                bank = tmp_bank(("sup", h))
                nc.vector.tensor_scalar(sup32[:, 8 * h:8 * h + 8, :], bank.rearrange("p (t d) -> p t d", d=D),
                                        SUP_SCALE, None, ALU.mult).then_inc(tmp_read, 1)
            dve.wait_ge(tmp_read, X_FILLS)
            split(sup32[:, :, :], sup[:, :, :], xb[:, :, :]).then_inc(sup_ready, 1)
            dve.wait_ge(sup_ready, 1)
            dve.wait_ge(par_loaded, 16 * 8)
            dve.wait_ge(x_loaded, 16)
            link(nc.vector.tensor_tensor(xb[:, :, :], xs[:, :, :],
                                         b0row[:, :].unsqueeze(1).to_broadcast([P, NB, D]), ALU.add))

            for i, g in enumerate(groups):
                p, bp, c = g
                if i == 2 * (NB // 2) + 2:
                    finish_layer0(0)
                    finish_layer0(1)
                if i == 2 * (NB // 2) + Y0_AT:
                    x1_transposed(0)
                    x1_transposed(1)
                    layer1_products(0)
                    layer1_products(1)
                bank = tmp_bank(("adj", g))
                i0 = (2 * p + c) * CH
                nc.vector.tensor_copy(adjT[:, 2 * bp:2 * bp + 2, i0:i0 + CH],
                                      bank.bitcast(BF16).rearrange("p (k n) -> p k n", k=2)).then_inc(tmp_read, 1)
            finish_layer0(2)
            finish_layer0(3)
            x1_transposed(2)
            x1_transposed(3)
            layer1_products(2)
            layer1_products(3)

            for g in range(NB // RT):
                t = g * RT
                bank = acc[:, (g % 2) * RT:(g % 2 + 1) * RT, :]
                dve.wait_ge(agg_done, g + 1)
                nc.vector.tensor_scalar(col[:, 6, :], bank[:, :, PD], 1.0, 1.0, ALU.add, ALU.max).then_inc(agg_read, 1)
                nc.vector.reduce_sum(t0[:, :, :], bank[:, :, 0:PD].rearrange("p t (k d) -> p t d k", k=PARTS),
                                     AX_X).then_inc(agg_read, 1)
                dve.wait_ge(agg_read, 2 * (g + 1))
                link(nc.vector.reciprocal(col[:, 7, :], col[:, 6, :]))
                link(nc.vector.tensor_tensor(t0[:, :, :], t0[:, :, :], yu[:, t:t + RT, 0, :], ALU.add))
                link(nc.vector.tensor_tensor(t0[:, :, :], t0[:, :, :], spread(col[:, 7, :]), ALU.mult))
                link(nc.vector.tensor_tensor(t0[:, :, :], t0[:, :, :], yu[:, t:t + RT, 1, :], ALU.add))
                link(nc.vector.tensor_scalar(t0[:, :, :], t0[:, :, :], 0.0, None, ALU.max))
                link(nc.vector.tensor_tensor(t1[:, :, :], t0[:, :, :], t0[:, :, :], ALU.mult))
                link(nc.vector.reduce_sum(col[:, 5, :], t1[:, :, :], AX_X))
                nc.vector.tensor_scalar(col[:, 0, :], col[:, 5, :], SS_MIN, None, ALU.max).then_inc(to_act, 1)
                newton_root()
                link(nc.vector.tensor_tensor(t0[:, :, :], t0[:, :, :], spread(col[:, 3, :]), ALU.mult))
                link(nc.vector.tensor_tensor(t0[:, :, :], t0[:, :, :], x1[:, t:t + RT, :], ALU.add))
                layernorm(t0, outs[:, t:t + RT, :]).then_inc(out_ready, 1)

        @block.tensor
        def _(pe):
            def tmp_bank(f):
                n = number[f]
                if n >= 2:
                    pe.wait_ge(tmp_read, n - 1)
                return tmp[:, n % 2, :]

            def transpose_adj(i):
                p, bp, c = groups[i]
                u = unit(p, bp, c)
                pe.wait_ge(adj_loaded[u % RING], 16 * (u // RING + 1))
                bank = tmp_bank(("adj", groups[i])).bitcast(BF16)
                halves = stage[:, u % RING, :, :].bitcast(BF16)
                for k in range(2):
                    for r in range(RT):
                        j0 = ((2 * bp + k) % QB) * P
                        last = nc.tensor.transpose(bank[:, k * CH + r * P:k * CH + (r + 1) * P],
                                                   halves[:, r, 2 * j0 + 1:2 * (j0 + P):2], ident16[:, :])
                last.then_inc(tmp_full, 1)

            def count(p, b, c):
                n = nth(p, b)
                i0 = (2 * p + c) * CH
                if n >= 1:
                    pe.wait_ge(w_ready[c], n)
                pe.wait_ge(tmp_read, number[("adj", (p, b // 2, c))] + 1)
                if b < NB - 1:
                    nc.tensor.matmul(cnt[:, c, :], rest[:, :], adjT[:, b + 1, i0:i0 + CH], start=False, stop=False,
                                     skip_group_check=True)
                nc.tensor.matmul(cnt[:, c, :], suffix[:, :], adjT[:, b, i0:i0 + CH], start=(b == NB - 1), stop=True,
                                 skip_group_check=True).then_inc(cnt_done[c], 1)

            def weigh(p, b, c):
                n = nth(p, b)
                pe.wait_ge(w_ready[c], n + 1)
                if n == 0:
                    pe.wait_ge(sup_ready, 1)
                if b == NB - 1 and p > 0:
                    pe.wait_ge(acc_read, 2 * (p - 1) + c + 1)
                for r in range(RT):
                    last = nc.tensor.matmul(acc[:, c * RT + r, 0:PD], wts[:, c, b % 2, r * P:(r + 1) * P],
                                            sup[:, b, :], start=(b == NB - 1 and r % 2 == 0), stop=(b == 0),
                                            skip_group_check=True)
                last.then_inc(w_used[c], 1)

            def transpose_x1(ch):
                pe.wait_ge(x1_ready, ch + 1)
                bank = tmp_bank(("x1T", ch))
                for k in range(2):
                    last = nc.tensor.transpose(bank[:, k * P:(k + 1) * P],
                                               x1[:, ch * RT + 2 * k:ch * RT + 2 * k + 2, :].rearrange("p t d -> p (t d)"),
                                               ident32[:, :])
                last.then_inc(tmp_full, 1)

            def multiply_x1(ch):
                pe.wait_ge(tmp_read, number[("x1T", ch)] + 1)
                bank = tmp_bank(("yu", ch))
                for k in range(2):
                    last = nc.tensor.matmul(bank[:, k * TS:(k + 1) * TS], x1T[:, 2 * ch + k, :],
                                            wd1[:, :, :, :].rearrange("p t s d -> p (t s d)"), start=True, stop=True)
                last.then_inc(tmp_full, 1)

            pe.wait_ge(consts, 6)
            pe.wait_ge(x_loaded, 16)
            for h in range(2):
                bank = tmp[:, h, :]
                for k in range(4):
                    t = 8 * h + 2 * k
                    last = nc.tensor.transpose(bank[:, k * P:(k + 1) * P],
                                               xs[:, t:t + 2, :].rearrange("p t d -> p (t d)"), ident32[:, :])
                last.then_inc(tmp_full, 1)
            pe.wait_ge(par_loaded, 16 * 8)
            for h in range(2):
                bank = tmp_bank(("sup", h))
                for k in range(4):
                    last = nc.tensor.matmul(bank[:, k * P:(k + 1) * P], xT[:, 4 * h + k, :],
                                            wd0[:, :, :].rearrange("p t d -> p (t d)"), start=True, stop=True)
                last.then_inc(tmp_full, 1)

            transpose_adj(0)
            transpose_adj(1)
            i = 2
            before = None
            for p in range(PAIRS):
                for b in reversed(range(NB)):
                    count(p, b, 0)
                    if before:
                        weigh(*before, 0)
                    if i < len(groups):
                        if i == 2 * (NB // 2) + Y0_AT:
                            transpose_x1(0)
                            transpose_x1(1)
                            multiply_x1(0)
                            multiply_x1(1)
                        transpose_adj(i)
                        i += 1
                    count(p, b, 1)
                    if before:
                        weigh(*before, 1)
                    before = (p, b)
            weigh(*before, 0)
            weigh(*before, 1)
            for ch in (2, 3):
                transpose_x1(ch)
            for ch in (2, 3):
                multiply_x1(ch)
            pe.wait_ge(y_ready, 4)
            for g in range(NB // RT):
                if g >= 2:
                    pe.wait_ge(agg_read, 2 * (g - 1))
                for r in range(RT):
                    for b in range(NB):
                        t = g * RT + r
                        last = nc.tensor.matmul(acc[:, (g % 2) * RT + r, 0:PD + 1], adjT[:, b, t * P:(t + 1) * P],
                                                ysp[:, b, 0:PD + 1], start=(b == 0 and r % 2 == 0),
                                                stop=(b == NB - 1), skip_group_check=True)
                last.then_inc(agg_done, 1)


_INS = ['x', 'adj', 'L0_gnn_weight', 'L0_gnn_bias', 'L1_gnn_W', 'L1_gnn_b']
_OUTS = [((N, D), 'float32')]


def kernel(**inputs):
    import numpy as _np
    import concourse.bacc as _bacc
    from concourse import mybir as _mybir
    from concourse.bass_utils import run_bass_kernel_spmd as _run

    nc = _bacc.Bacc("TRN2", target_bir_lowering=False, num_devices=1)
    arrays, args = {}, []
    for name in _INS:
        a = _np.ascontiguousarray(inputs[name])
        arrays[f"in_{name}_dram"] = a
        args.append(nc.dram_tensor(f"in_{name}_dram", a.shape, _mybir.dt.from_np(a.dtype), kind="ExternalInput").ap())
    for i, (shape, dtype) in enumerate(_OUTS):
        dt = _mybir.dt.from_np(_np.dtype(dtype))
        args.append(nc.dram_tensor(f"out_{i}_dram", shape, dt, kind="ExternalOutput").ap())
    build(nc, *args)
    r = _run(nc, [arrays], core_ids=[0])
    return r.results[0]["out_0_dram"]
```

```python
from contextlib import ExitStack

import concourse.bass as bass
from concourse import mybir

P = 128
N, D = 2048, 64
NB = N // P
PARTS = 3
PD = PARTS * D
CH = 512
RT = CH // P
PAIRS = N // (2 * CH)
QB = 4
UNITS = 2 * NB // QB
RING = 8
WRING = 4
LAG = 3
PT = 2 * RT
SECOND = NB
FINISH = SECOND + LAG + 1
TS = 256
NEIGH = 100
EXP1 = 128
LN_EPS = 1e-5
SS_MIN = 1e-24
SUP_SCALE = 2.0 ** (127 - NEIGH)

LAYER1 = [(0, 0), (0, 1), (1, 0), (0, 2), (0, 3), (1, 1), (0, 4), (1, 2), (0, 5), (1, 3), (1, 4), (1, 5)]
LAST = 1

ALU = mybir.AluOpType
ACT = mybir.ActivationFunctionType
AX_X = mybir.AxisListType.X
F32 = mybir.dt.float32
BF16 = mybir.dt.bfloat16
I16 = mybir.dt.int16


def build(nc, x, adj, w0, b0, w1, b1, out):
    with ExitStack() as ctx:
        def sb(name, shape, dt):
            return ctx.enter_context(nc.sbuf_tensor(name, shape, dt))

        def psum(name, shape, dt):
            return ctx.enter_context(nc.psum_tensor(name, shape, dt))

        def sem(name):
            return ctx.enter_context(nc.semaphore(name))

        stage = sb("stage", [P, RING, RT, QB * P], F32)
        adjT = sb("adjT", [P, NB, N], BF16)
        wts = sb("wts", [P, 2, WRING, CH], BF16)
        xs = sb("xs", [P, NB, D], F32)
        xb = sb("xb", [P, NB, D], F32)
        xT = sb("xT", [P, NB // 2, P], F32)
        sup32 = sb("sup32", [P, NB, D], F32)
        left32 = sb("left32", [P, NB, D], F32)
        sup = sb("sup", [P, NB, PD], BF16)
        x1 = sb("x1", [P, NB, D], F32)
        x1T = sb("x1T", [P, PT // 2, P], F32)
        yu = sb("yu", [P, NB, 2, D], F32)
        ysp = sb("ysp", [P, NB, PD + 2], BF16)
        suffix = sb("suffix", [P, P], BF16)
        rest = sb("rest", [P, P], BF16)
        ident16 = sb("ident16", [P, P], BF16)
        ident32 = sb("ident32", [P, P], F32)
        wd0 = sb("wd0", [P, 2, D], F32)
        wd1 = sb("wd1", [P, 2, 2, D], F32)
        b0row = sb("b0row", [P, D], F32)
        b1row = sb("b1row", [P, D], F32)
        t0 = sb("t0", [P, 2 * PT, D], F32)
        t1 = sb("t1", [P, 2 * PT, D], F32)
        t2 = sb("t2", [P, 2 * PT, D], F32)
        var = sb("var", [P, 2, 2 * PT], F32)
        root = sb("root", [P, 2, 2 * PT], F32)
        small = sb("small", [P, 4, 2 * PT], F32)
        outs = sb("outs", [P, NB, D], F32)

        acc = psum("acc", [P, PT, TS], F32)
        tmp = psum("tmp", [P, 2, CH], F32)
        cnt = psum("cnt", [P, 2, CH], F32)
        agg = [cnt[:, :, :].rearrange("p b (h n) -> p (b h) n", h=2), acc[:, 0:RT, :], acc[:, RT:PT, :],
               tmp[:, :, :].rearrange("p b (h n) -> p (b h) n", h=2)]

        x_loaded = [sem(f"x_loaded{h}") for h in range(2)]
        w0_loaded = sem("w0_loaded")
        par_loaded = sem("par_loaded")
        adj_loaded = [sem(f"adj_loaded{i}") for i in range(RING)]
        wd_zeroed = sem("wd_zeroed")
        zeroed = sem("zeroed")
        ident32_ready = sem("ident32_ready")
        consts = sem("consts")
        xT_done = sem("xT_done")
        xT_ready = sem("xT_ready")
        sup_done = sem("sup_done")
        sup_steps = sem("sup_steps")
        sup_left = sem("sup_left")
        biased = sem("biased")
        scaled = sem("scaled")
        added = sem("added")
        squared = sem("squared")
        normed = sem("normed")
        summed = sem("summed")
        centred = sem("centred")
        spreads = sem("spreads")
        sup_ready = sem("sup_ready")
        tmp_full = sem("tmp_full")
        tmp_read = sem("tmp_read")
        cnt_done = [sem(f"cnt_done{i}") for i in range(2)]
        w_ready = [sem(f"w_ready{i}") for i in range(2)]
        w_used = [sem(f"w_used{i}") for i in range(2)]
        acc_read = sem("acc_read")
        x1_ready = sem("x1_ready")
        y_ready = sem("y_ready")
        diag_ready = sem("diag_ready")
        agg_done = sem("agg_done")
        chain = sem("chain")
        to_root = sem("to_root")
        rooted = sem("rooted")
        out_ready = sem("out_ready")
        stored = sem("stored")

        groups = [(p, NB // 2 - 1 - k, c) for p in range(PAIRS) for k in range(NB // 2) for c in range(2)]
        fills = []
        for i, g in enumerate(groups):
            if i == FINISH + 5:
                fills += [("x1T", 0)]
            if i == FINISH + 6:
                fills += [("yu", 0, 0), ("yu", 0, 1)]
            fills.append(("adj", g))
        fills += [("x1T", 1), ("yu", 1, 0), ("yu", 1, 1)]
        number = {f: i for i, f in enumerate(fills)}

        def unit(p, bp, c):
            return p * UNITS + (NB // QB - 1 - bp // 2) * 2 + c

        def nth(p, b):
            return p * NB + NB - 1 - b

        x_v = x.rearrange("(t p) d -> p t d", p=P)
        out_v = out.rearrange("(t p) d -> p t d", p=P)
        adj_v = adj.rearrange("(c r p) (q n) -> c q p r n", r=RT, p=P, n=QB * P)

        block = ctx.enter_context(nc.Block())

        @block.sync
        def _(sp):
            for h in (1, 0):
                sp.dma_start(xs[:, h * PT:(h + 1) * PT, :], x_v[:, h * PT:(h + 1) * PT, :]).then_inc(x_loaded[h], 16)
            for p in range(PAIRS):
                for q in range(NB // QB):
                    for c in range(2):
                        u = p * UNITS + 2 * q + c
                        if u >= RING:
                            v = u - RING
                            old = (v // UNITS, 2 * (NB // QB - 1 - v % UNITS // 2), v % 2)
                            sp.wait_ge(tmp_full, number[("adj", old)] + 1)
                        sp.dma_start(stage[:, u % RING, :, :],
                                     adj_v[2 * p + c, NB // QB - 1 - q]).then_inc(adj_loaded[u % RING], 16)
            for g in range(2):
                sp.wait_ge(out_ready, g + 1)
                sp.dma_start(out_v[:, g * PT:(g + 1) * PT, :],
                             outs[:, g * PT:(g + 1) * PT, :]).then_inc(stored, 16)
            sp.wait_ge(stored, 32)

        @block.gpsimd
        def _(pool):
            nc.gpsimd.memset(ident32[:], 0.0).then_inc(zeroed, 1)
            nc.gpsimd.memset(ident16[:], 0.0).then_inc(zeroed, 1)
            nc.gpsimd.memset(suffix[:], -float(EXP1)).then_inc(zeroed, 1)
            nc.gpsimd.memset(rest[:], -float(EXP1)).then_inc(zeroed, 1)

            def select(t, op, fill, s=1):
                return nc.gpsimd.affine_select(out=t[:, :], in_=t[:, :], compare_op=op, fill=fill, base=0,
                                               pattern=[[-s, P]], channel_multiplier=s)
            pool.wait_ge(zeroed, 4)
            select(ident32, ALU.not_equal, 1.0).then_inc(ident32_ready, 1)
            select(ident16, ALU.not_equal, 1.0).then_inc(consts, 1)
            pool.wait_ge(consts, 1)
            select(suffix, ALU.is_ge, 0.0).then_inc(consts, 1)
            select(rest, ALU.is_ge, 0.0, -1).then_inc(consts, 1)
            pool.wait_ge(consts, 3)
            select(suffix, ALU.not_equal, float(EXP1 * NEIGH)).then_inc(consts, 1)
            select(rest, ALU.not_equal, -float(EXP1 * (NEIGH + 1))).then_inc(consts, 1)
            nc.gpsimd.memset(ysp[:, :, PD:PD + 2], 1.0).then_inc(consts, 1)
            for p in range(PAIRS):
                for c in range(2):
                    pool.wait_ge(cnt_done[c], (p + 1) * NB)
                for b in range(p * PT, (p + 1) * PT):
                    d = adjT[:, b, b * P:(b + 1) * P]
                    nc.gpsimd.tensor_tensor(d, d, ident16[:, :], ALU.add).then_inc(diag_ready, 1)

                pool.wait_ge(tmp_read, number[("yu", p, 1)] + 1)
                u = yu[:, p * PT:(p + 1) * PT, 1, :]
                nc.gpsimd.tensor_tensor(u, u, b1row[:, :].unsqueeze(1).to_broadcast([P, PT, D]),
                                        ALU.add).then_inc(biased, 1)
            pool.wait_ge(biased, PAIRS)
            for g, step in LAYER1:
                v = slice(PT * g, PT * g + PT)
                if step == 0:
                    pool.wait_ge(scaled, g + 1)
                    nc.gpsimd.tensor_tensor(t0[:, v, :], t0[:, v, :], yu[:, v, 1, :], ALU.add).then_inc(added, 1)
                if step == 2 and g < LAST:
                    pool.wait_ge(normed, g + 1)
                    nc.gpsimd.tensor_tensor(t0[:, v, :], t0[:, v, :], x1[:, v, :], ALU.add).then_inc(summed, 1)

        @block.scalar
        def _(act):
            act.wait_ge(wd_zeroed, 2)
            for h in range(2):
                act.dma_start(wd0[h * D:(h + 1) * D, h, :], w0).then_inc(w0_loaded, 16)
            act.dma_start(b0row[:, :], b0.partition_broadcast(P)).then_inc(par_loaded, 16)
            act.dma_start(b1row[:, :], b1.partition_broadcast(P)).then_inc(par_loaded, 16)
            for h in range(2):
                act.dma_start(wd1[h * D:(h + 1) * D, h, 0, :], w1[D:2 * D, :]).then_inc(par_loaded, 16)
                act.dma_start(wd1[h * D:(h + 1) * D, h, 1, :], w1[0:D, :]).then_inc(par_loaded, 16)
            for k, h in enumerate((1, 0)):
                act.wait_ge(xT_done, k + 1)
                nc.scalar.copy(xT[:, 4 * h:4 * h + 4, :],
                               acc[:, 2 * h:2 * h + 2, :].rearrange("p a (b n) -> p (a b) n", n=P)).then_inc(xT_ready, 1)
            for k, h in enumerate((1, 0)):
                v = slice(h * PT, (h + 1) * PT)
                act.wait_ge(sup_done, k + 1)
                nc.scalar.activation(sup32[:, v, :], acc[:, 4 + 2 * h:6 + 2 * h, :].rearrange("p a (b d) -> p (a b) d", d=D),
                                     ACT.Copy, scale=SUP_SCALE).then_inc(sup_steps, 1)
                act.wait_ge(sup_steps, 3 * k + 1)
                nc.scalar.copy(sup[:, v, 0:D], sup32[:, v, :]).then_inc(sup_steps, 1)
                act.wait_ge(sup_left, k + 1)
                nc.scalar.copy(sup[:, v, D:2 * D], left32[:, v, :]).then_inc(sup_steps, 1)

            def take_root(n, k, v):
                act.wait_ge(to_root, n + 1)
                nc.scalar.activation(root[:, k, v], var[:, k, v], ACT.Sqrt).then_inc(rooted, 1)

            for p in range(PAIRS):
                for b in reversed(range(NB)):
                    for c in range(2):
                        n = nth(p, b)
                        act.wait_ge(cnt_done[c], n + 1)
                        if n >= WRING:
                            act.wait_ge(w_used[c], n - WRING + 1)
                        nc.scalar.activation(wts[:, c, b % WRING, :].bitcast(I16), cnt[:, c, :],
                                             ACT.Relu).then_inc(w_ready[c], 1)
                    if p == 1 and b == NB - 3 - LAG:
                        take_root(0, 0, slice(0, PT))
            take_root(1, 0, slice(0, PT))
            n = 2
            for g, step in LAYER1:
                v = slice(PT * g, PT * g + PT)
                if step == 0:
                    act.wait_ge(added, g + 1)
                    nc.scalar.activation(t1[:, v, :], t0[:, v, :], ACT.Relu).then_inc(squared, 1)
                    act.wait_ge(squared, 2 * g + 1)
                    nc.scalar.activation(t2[:, v, :], t1[:, v, :], ACT.Square).then_inc(squared, 1)
                if step == 1 or step == 4:
                    take_root(n, 1 if step == 1 else 0, v)
                    n += 1
                if step == 3:
                    act.wait_ge(centred, g + 1)
                    nc.scalar.activation(t1[:, v, :], t2[:, v, :], ACT.Square).then_inc(spreads, 1)

        @block.vector
        def _(dve):
            steps = [0]

            def link(ins):
                steps[0] += 1
                ins.then_inc(chain, 1)
                dve.wait_ge(chain, steps[0])

            roots = [0]

            def tmp_bank(f):
                n = number[f]
                dve.wait_ge(tmp_full, n + 1)
                return tmp[:, n % 2, :]

            def spread(v):
                return v.unsqueeze(2).to_broadcast([P, v.shape[1], D])

            def inverse_root(k, v):
                roots[0] += 1
                dve.wait_ge(rooted, roots[0])
                y, h = small[:, 2, v], small[:, 3, v]
                link(nc.vector.reciprocal(y, root[:, k, v]))
                link(nc.vector.tensor_tensor(h, y, y, ALU.mult))
                link(nc.vector.scalar_tensor_tensor(out=h, in0=h, scalar=-0.5, in1=var[:, k, v],
                                                    op0=ALU.mult, op1=ALU.mult))
                link(nc.vector.scalar_tensor_tensor(out=h, in0=h, scalar=1.5, in1=y, op0=ALU.add, op1=ALU.mult))
                return spread(h)

            def center(v):
                link(nc.vector.reduce_sum(small[:, 0, v], t0[:, v, :], AX_X))
                link(nc.vector.scalar_tensor_tensor(out=t2[:, v, :], in0=spread(small[:, 0, v]), scalar=-1.0 / D,
                                                    in1=t0[:, v, :], op0=ALU.mult, op1=ALU.add))

            def variance(k, v):
                link(nc.vector.tensor_tensor(t1[:, v, :], t2[:, v, :], t2[:, v, :], ALU.mult))
                link(nc.vector.reduce_sum(small[:, 1, v], t1[:, v, :], AX_X))
                nc.vector.tensor_scalar(var[:, k, v], small[:, 1, v], 1.0 / D, LN_EPS,
                                        ALU.mult, ALU.add).then_inc(to_root, 1)

            def finish_layer0(p, step):
                v, w = slice(0, PT), slice(p * PT, (p + 1) * PT)
                if step == 0:
                    for c in range(2):
                        dve.wait_ge(w_used[c], (p + 1) * NB)
                        sums = acc[:, c * RT:(c + 1) * RT, 0:PD].rearrange("p t (k d) -> p t d k", k=PARTS)
                        nc.vector.reduce_sum(t0[:, c * RT:(c + 1) * RT, :], sums, AX_X).then_inc(acc_read, 1)
                if step == 1:
                    dve.wait_ge(acc_read, 2 * p + 2)
                    link(nc.vector.tensor_tensor(t0[:, v, :], t0[:, v, :], xb[:, w, :], ALU.add))
                    center(v)
                if step == 2:
                    variance(0, v)
                if step == 4:
                    r = inverse_root(0, v)
                    nc.vector.tensor_tensor(x1[:, w, :], t2[:, v, :], r, ALU.mult).then_inc(x1_ready, 1)
                if step == 5:
                    bank = tmp_bank(("x1T", p))
                    nc.vector.tensor_copy(x1T[:, :, :], bank.rearrange("p (k n) -> p k n", k=4)).then_inc(tmp_read, 1)
                if step == 6:
                    for h in range(2):
                        bank = tmp_bank(("yu", p, h))
                        t = p * PT + h * RT
                        nc.vector.tensor_copy(yu[:, t:t + RT, :, :],
                                              bank.rearrange("p (t s d) -> p t s d", t=RT, s=2)).then_inc(tmp_read, 1)
                    dve.wait_ge(tmp_read, number[("yu", p, 1)] + 1)
                if step == 7:
                    link(nc.vector.tensor_copy(ysp[:, w, 0:D], yu[:, w, 0, :]))
                    link(nc.vector.tensor_tensor(t0[:, v, :], yu[:, w, 0, :], ysp[:, w, 0:D], ALU.subtract))
                    link(nc.vector.tensor_copy(ysp[:, w, D:2 * D], t0[:, v, :]))
                    nc.vector.tensor_tensor(ysp[:, w, 2 * D:3 * D], t0[:, v, :], ysp[:, w, D:2 * D],
                                            ALU.subtract).then_inc(y_ready, 1)

            nc.vector.memset(wd0[:], 0.0).then_inc(wd_zeroed, 1)
            nc.vector.memset(wd1[:], 0.0).then_inc(wd_zeroed, 1)
            for i, g in enumerate(groups):
                p, bp, c = g
                if i in (1, 3):
                    k = i // 2
                    v = slice((1 - k) * PT, (2 - k) * PT)
                    dve.wait_ge(sup_steps, 3 * k + 2)
                    nc.vector.tensor_tensor(left32[:, v, :], sup32[:, v, :], sup[:, v, 0:D],
                                            ALU.subtract).then_inc(sup_left, 1)
                    dve.wait_ge(sup_steps, 3 * k + 3)
                    nc.vector.tensor_tensor(sup[:, v, 2 * D:3 * D], left32[:, v, :], sup[:, v, D:2 * D],
                                            ALU.subtract).then_inc(sup_ready, 1)
                if i == 6:
                    dve.wait_ge(par_loaded, 16 * 6)
                    dve.wait_ge(x_loaded[0], 16)
                    dve.wait_ge(x_loaded[1], 16)
                    link(nc.vector.tensor_tensor(xb[:, :, :], xs[:, :, :],
                                                 b0row[:, :].unsqueeze(1).to_broadcast([P, NB, D]), ALU.add))
                if i >= FINISH:
                    finish_layer0(0, i - FINISH)
                bank = tmp_bank(("adj", g))
                i0 = (2 * p + c) * CH
                nc.vector.tensor_copy(adjT[:, 2 * bp:2 * bp + 2, i0:i0 + CH],
                                      bank.bitcast(BF16).rearrange("p (k n) -> p k n", k=2)).then_inc(tmp_read, 1)
            for step in range(8):
                finish_layer0(1, step)

            def layer1(g, step):
                v = slice(PT * g, PT * g + PT)
                a, b, c = t0[:, v, :], t1[:, v, :], t2[:, v, :]
                if step == 0:
                    for q in (2 * g, 2 * g + 1):
                        u = slice(RT * q, RT * q + RT)
                        dve.wait_ge(agg_done, q + 1)
                        nc.vector.tensor_scalar(small[:, 2, u], agg[q][:, :, PD], 1.0, None,
                                                ALU.max).then_inc(chain, 1)
                        nc.vector.reduce_sum(t0[:, u, :], agg[q][:, :, 0:PD].rearrange("p t (k d) -> p t d k", k=PARTS),
                                             AX_X).then_inc(chain, 1)
                    steps[0] += 4
                    dve.wait_ge(chain, steps[0])
                    link(nc.vector.reciprocal(small[:, 3, v], small[:, 2, v]))
                    nc.vector.tensor_tensor(a, a, spread(small[:, 3, v]), ALU.mult).then_inc(scaled, 1)
                if step == 1:
                    dve.wait_ge(squared, 2 * g + 2)
                    link(nc.vector.reduce_sum(small[:, 0, v], c, AX_X))
                    nc.vector.tensor_scalar(var[:, 1, v], small[:, 0, v], SS_MIN, None, ALU.max).then_inc(to_root, 1)
                if step == 2:
                    r = inverse_root(1, v)
                    nc.vector.tensor_tensor(a, b, r, ALU.mult).then_inc(normed, 1)
                if step == 3:
                    if g == LAST:
                        dve.wait_ge(normed, g + 1)
                        link(nc.vector.tensor_tensor(a, a, x1[:, v, :], ALU.add))
                    else:
                        dve.wait_ge(summed, g + 1)
                    link(nc.vector.reduce_sum(small[:, 0, v], a, AX_X))
                    nc.vector.scalar_tensor_tensor(out=c, in0=spread(small[:, 0, v]), scalar=-1.0 / D, in1=a,
                                                   op0=ALU.mult, op1=ALU.add).then_inc(centred, 1)
                if step == 4:
                    dve.wait_ge(spreads, g + 1)
                    link(nc.vector.reduce_sum(small[:, 1, v], b, AX_X))
                    nc.vector.tensor_scalar(var[:, 0, v], small[:, 1, v], 1.0 / D, LN_EPS,
                                            ALU.mult, ALU.add).then_inc(to_root, 1)
                if step == 5:
                    dve.wait_ge(centred, g + 1)
                    r = inverse_root(0, v)
                    nc.vector.tensor_tensor(outs[:, v, :], c, r, ALU.mult).then_inc(out_ready, 1)

            for g, step in LAYER1:
                layer1(g, step)

        @block.tensor
        def _(pe):
            def tmp_bank(f):
                n = number[f]
                if n >= 2:
                    pe.wait_ge(tmp_read, n - 1)
                return tmp[:, n % 2, :]

            def transpose_adj(i):
                p, bp, c = groups[i]
                u = unit(p, bp, c)
                pe.wait_ge(adj_loaded[u % RING], 16 * (u // RING + 1))
                bank = tmp_bank(("adj", groups[i])).bitcast(BF16)
                halves = stage[:, u % RING, :, :].bitcast(BF16)
                for k in range(2):
                    for r in range(RT):
                        j0 = ((2 * bp + k) % QB) * P
                        last = nc.tensor.transpose(bank[:, k * CH + r * P:k * CH + (r + 1) * P],
                                                   halves[:, r, 2 * j0 + 1:2 * (j0 + P):2], ident16[:, :])
                last.then_inc(tmp_full, 1)

            def count(p, b, c):
                n = nth(p, b)
                i0 = (2 * p + c) * CH
                if n >= 1:
                    pe.wait_ge(w_ready[c], n)
                pe.wait_ge(tmp_read, number[("adj", (p, b // 2, c))] + 1)
                if b < NB - 1:
                    nc.tensor.matmul(cnt[:, c, :], rest[:, :], adjT[:, b + 1, i0:i0 + CH], start=False, stop=False,
                                     skip_group_check=True)
                nc.tensor.matmul(cnt[:, c, :], suffix[:, :], adjT[:, b, i0:i0 + CH], start=(b == NB - 1), stop=True,
                                 skip_group_check=True).then_inc(cnt_done[c], 1)

            def weigh(p, b, c):
                n = nth(p, b)
                pe.wait_ge(w_ready[c], n + 1)
                if p == 0 and b in (NB - 1, PT - 1):
                    pe.wait_ge(sup_ready, 1 if b >= PT else 2)
                if b == NB - 1 and p > 0:
                    pe.wait_ge(acc_read, 2 * (p - 1) + c + 1)
                for r in range(RT):
                    last = nc.tensor.matmul(acc[:, c * RT + r, 0:PD], wts[:, c, b % WRING, r * P:(r + 1) * P],
                                            sup[:, b, :], start=(b == NB - 1 and r % 2 == 0), stop=(b == 0),
                                            skip_group_check=True)
                last.then_inc(w_used[c], 1)

            def transpose_x1(p):
                pe.wait_ge(x1_ready, p + 1)
                bank = tmp_bank(("x1T", p))
                for k in range(4):
                    t = p * PT + 2 * k
                    last = nc.tensor.transpose(bank[:, k * P:(k + 1) * P],
                                               x1[:, t:t + 2, :].rearrange("p t d -> p (t d)"), ident32[:, :])
                last.then_inc(tmp_full, 1)

            def multiply_x1(p):
                pe.wait_ge(par_loaded, 16 * 6)
                pe.wait_ge(tmp_read, number[("x1T", p)] + 1)
                for h in range(2):
                    bank = tmp_bank(("yu", p, h))
                    for k in range(2):
                        last = nc.tensor.matmul(bank[:, k * TS:(k + 1) * TS], x1T[:, 2 * h + k, :],
                                                wd1[:, :, :, :].rearrange("p t s d -> p (t s d)"),
                                                start=True, stop=True)
                    last.then_inc(tmp_full, 1)

            def aggregate(g, half):
                for r in range(RT):
                    t = g * RT + r
                    for b in range(half * PT, half * PT + PT):
                        last = nc.tensor.matmul(agg[g][:, r, 0:PD + 1], adjT[:, b, t * P:(t + 1) * P],
                                                ysp[:, b, 0:PD + 1], start=(b == 0 and r % 2 == 0),
                                                stop=(b == NB - 1), skip_group_check=True)
                if half == 1:
                    last.then_inc(agg_done, 1)

            pe.wait_ge(ident32_ready, 1)
            for n, h in enumerate((1, 0)):
                pe.wait_ge(x_loaded[h], 16)
                for k in range(4):
                    t = h * PT + 2 * k
                    last = nc.tensor.transpose(acc[:, 2 * h + k // 2, (k % 2) * P:(k % 2 + 1) * P],
                                               xs[:, t:t + 2, :].rearrange("p t d -> p (t d)"), ident32[:, :])
                last.then_inc(xT_done, 1)
            pe.wait_ge(consts, 1)
            transpose_adj(0)
            pe.wait_ge(w0_loaded, 32)
            for n, h in enumerate((1, 0)):
                pe.wait_ge(xT_ready, n + 1)
                for k in range(4):
                    last = nc.tensor.matmul(acc[:, 4 + 2 * h + k // 2, (k % 2) * P:(k % 2 + 1) * P],
                                            xT[:, 4 * h + k, :], wd0[:, :, :].rearrange("p t d -> p (t d)"),
                                            start=True, stop=True)
                last.then_inc(sup_done, 1)
            transpose_adj(1)
            pe.wait_ge(consts, 6)

            blocks = [(p, b) for p in range(PAIRS) for b in reversed(range(NB))]
            for n, (p, b) in enumerate(blocks):
                for c in range(2):
                    count(p, b, c)
                    if n >= LAG:
                        weigh(*blocks[n - LAG], c)
                    if c == 0 and n + 2 < len(groups):
                        if n + 2 == FINISH + 5:
                            transpose_x1(0)
                        if n + 2 == FINISH + 6:
                            multiply_x1(0)
                        transpose_adj(n + 2)
            for n in range(len(blocks) - LAG, len(blocks)):
                weigh(*blocks[n], 0)
                weigh(*blocks[n], 1)
            pe.wait_ge(y_ready, 1)
            pe.wait_ge(diag_ready, PT)
            aggregate(0, 0)
            pe.wait_ge(acc_read, 2 * PAIRS)
            aggregate(1, 0)
            aggregate(2, 0)
            transpose_x1(1)
            multiply_x1(1)
            pe.wait_ge(tmp_read, len(fills))
            aggregate(3, 0)
            pe.wait_ge(y_ready, 2)
            pe.wait_ge(diag_ready, NB)
            for g in range(NB // RT):
                aggregate(g, 1)


_INS = ['x', 'adj', 'L0_gnn_weight', 'L0_gnn_bias', 'L1_gnn_W', 'L1_gnn_b']
_OUTS = [((N, D), 'float32')]


def kernel(**inputs):
    import numpy as _np
    import concourse.bacc as _bacc
    from concourse import mybir as _mybir
    from concourse.bass_utils import run_bass_kernel_spmd as _run

    nc = _bacc.Bacc("TRN2", target_bir_lowering=False, num_devices=1)
    arrays, args = {}, []
    for name in _INS:
        a = _np.ascontiguousarray(inputs[name])
        arrays[f"in_{name}_dram"] = a
        args.append(nc.dram_tensor(f"in_{name}_dram", a.shape, _mybir.dt.from_np(a.dtype), kind="ExternalInput").ap())
    for i, (shape, dtype) in enumerate(_OUTS):
        dt = _mybir.dt.from_np(_np.dtype(dtype))
        args.append(nc.dram_tensor(f"out_{i}_dram", shape, dt, kind="ExternalOutput").ap())
    build(nc, *args)
    r = _run(nc, [arrays], core_ids=[0])
    return r.results[0]["out_0_dram"]
```
